# Optimizing a Trainium2 kernel written in Bass

```python
import numpy as np
import jax
import jax.numpy as jnp

def _softmax(x, axis=-1):
    return jax.nn.softmax(x, axis=axis)

def _gelu(x):
    return jax.nn.gelu(x, approximate=True)

def _silu(x):
    return jax.nn.silu(x)

def _sigmoid(x):
    return jax.nn.sigmoid(x)

def _layernorm(x, axis=-1, eps=1e-05):
    m = jnp.mean(x, axis=axis, keepdims=True)
    v = jnp.var(x, axis=axis, keepdims=True)
    return (x - m) / jnp.sqrt(v + eps)

def _scatter_add(tgt, idx, src, axis=0):
    return tgt.at[idx].add(src)

def _segment_sum(src, seg, n):
    return jax.ops.segment_sum(src, seg, n)
kernel_name = 'mk_dlrm_tower_d1_rec_r8_7e8e0f'

def setup_inputs(seed: int=0):
    np.random.seed(seed)
    _w = jnp.asarray

    def _rec_inputs():
        import jax
        import jax.numpy as jnp
        _tk = jax.random.key(seed)
        ids = jnp.stack([jax.random.randint(jax.random.fold_in(_tk, 200 + f), (512,), 0, v, jnp.int32) for f, v in enumerate([12500, 1000, 12500, 1250, 1250, 12500, 125000, 12500, 1000, 1250, 12500, 1250, 1000, 12500, 12500, 1250, 12500, 1000, 1000, 1000, 1250, 1250, 1250, 1250, 1000, 1000])], axis=1)
        tbl_0 = 0.05 * jax.random.normal(jax.random.fold_in(_tk, 500 + 0), (12500, 128), jnp.float32)
        tbl_1 = 0.05 * jax.random.normal(jax.random.fold_in(_tk, 500 + 1), (1000, 128), jnp.float32)
        tbl_2 = 0.05 * jax.random.normal(jax.random.fold_in(_tk, 500 + 2), (12500, 128), jnp.float32)
        tbl_3 = 0.05 * jax.random.normal(jax.random.fold_in(_tk, 500 + 3), (1250, 128), jnp.float32)
        tbl_4 = 0.05 * jax.random.normal(jax.random.fold_in(_tk, 500 + 4), (1250, 128), jnp.float32)
        tbl_5 = 0.05 * jax.random.normal(jax.random.fold_in(_tk, 500 + 5), (12500, 128), jnp.float32)
        tbl_6 = 0.05 * jax.random.normal(jax.random.fold_in(_tk, 500 + 6), (125000, 128), jnp.float32)
        tbl_7 = 0.05 * jax.random.normal(jax.random.fold_in(_tk, 500 + 7), (12500, 128), jnp.float32)
        tbl_8 = 0.05 * jax.random.normal(jax.random.fold_in(_tk, 500 + 8), (1000, 128), jnp.float32)
        tbl_9 = 0.05 * jax.random.normal(jax.random.fold_in(_tk, 500 + 9), (1250, 128), jnp.float32)
        tbl_10 = 0.05 * jax.random.normal(jax.random.fold_in(_tk, 500 + 10), (12500, 128), jnp.float32)
        tbl_11 = 0.05 * jax.random.normal(jax.random.fold_in(_tk, 500 + 11), (1250, 128), jnp.float32)
        tbl_12 = 0.05 * jax.random.normal(jax.random.fold_in(_tk, 500 + 12), (1000, 128), jnp.float32)
        tbl_13 = 0.05 * jax.random.normal(jax.random.fold_in(_tk, 500 + 13), (12500, 128), jnp.float32)
        tbl_14 = 0.05 * jax.random.normal(jax.random.fold_in(_tk, 500 + 14), (12500, 128), jnp.float32)
        tbl_15 = 0.05 * jax.random.normal(jax.random.fold_in(_tk, 500 + 15), (1250, 128), jnp.float32)
        tbl_16 = 0.05 * jax.random.normal(jax.random.fold_in(_tk, 500 + 16), (12500, 128), jnp.float32)
        tbl_17 = 0.05 * jax.random.normal(jax.random.fold_in(_tk, 500 + 17), (1000, 128), jnp.float32)
        tbl_18 = 0.05 * jax.random.normal(jax.random.fold_in(_tk, 500 + 18), (1000, 128), jnp.float32)
        tbl_19 = 0.05 * jax.random.normal(jax.random.fold_in(_tk, 500 + 19), (1000, 128), jnp.float32)
        tbl_20 = 0.05 * jax.random.normal(jax.random.fold_in(_tk, 500 + 20), (1250, 128), jnp.float32)
        tbl_21 = 0.05 * jax.random.normal(jax.random.fold_in(_tk, 500 + 21), (1250, 128), jnp.float32)
        tbl_22 = 0.05 * jax.random.normal(jax.random.fold_in(_tk, 500 + 22), (1250, 128), jnp.float32)
        tbl_23 = 0.05 * jax.random.normal(jax.random.fold_in(_tk, 500 + 23), (1250, 128), jnp.float32)
        tbl_24 = 0.05 * jax.random.normal(jax.random.fold_in(_tk, 500 + 24), (1000, 128), jnp.float32)
        tbl_25 = 0.05 * jax.random.normal(jax.random.fold_in(_tk, 500 + 25), (1000, 128), jnp.float32)
        _rk = jax.random.fold_in(_tk, 7)
        r_dense_features = -0.000520686 + 1.00062 * jax.random.normal(jax.random.fold_in(_rk, 101), (512, 128), jnp.float32)
        W_top1 = 0.0405887 * jax.random.normal(jax.random.fold_in(_tk, 801), (607, 512), jnp.float32)
        W_top2 = 0.0441942 * jax.random.normal(jax.random.fold_in(_tk, 802), (512, 256), jnp.float32)
        W_top3 = 0.0625 * jax.random.normal(jax.random.fold_in(_tk, 803), (256, 1), jnp.float32)
        b_top1 = jnp.zeros((512,), jnp.float32)
        b_top2 = jnp.zeros((256,), jnp.float32)
        return (r_dense_features, ids, tbl_0, tbl_1, tbl_2, tbl_3, tbl_4, tbl_5, tbl_6, tbl_7, tbl_8, tbl_9, tbl_10, tbl_11, tbl_12, tbl_13, tbl_14, tbl_15, tbl_16, tbl_17, tbl_18, tbl_19, tbl_20, tbl_21, tbl_22, tbl_23, tbl_24, tbl_25, W_top1, b_top1, W_top2, b_top2, W_top3)
    r_dense_features, ids, tbl_0, tbl_1, tbl_2, tbl_3, tbl_4, tbl_5, tbl_6, tbl_7, tbl_8, tbl_9, tbl_10, tbl_11, tbl_12, tbl_13, tbl_14, tbl_15, tbl_16, tbl_17, tbl_18, tbl_19, tbl_20, tbl_21, tbl_22, tbl_23, tbl_24, tbl_25, W_top1, b_top1, W_top2, b_top2, W_top3 = _rec_inputs()

    def _L0_rec_setup():
        import jax, jax.numpy as jnp
        import numpy as np
        F = 26
        key = jax.random.key(seed)
        k1, k2 = jax.random.split(key)
        B, D = (2048, 128)
        dense_features = jax.random.normal(k1, (B, D), dtype=jnp.float32)
        sparse_features = jax.random.normal(k2, (B, F, D), dtype=jnp.float32)
        return {'dense_features': dense_features, 'sparse_features': sparse_features}
    _L0_rec_all = _L0_rec_setup()
    _L0_rec_in = {k: v for k, v in _L0_rec_all.items() if k in ()}
    del _L0_rec_all
    return {'r_dense_features': r_dense_features, 'ids': ids, 'tbl_0': tbl_0, 'tbl_1': tbl_1, 'tbl_2': tbl_2, 'tbl_3': tbl_3, 'tbl_4': tbl_4, 'tbl_5': tbl_5, 'tbl_6': tbl_6, 'tbl_7': tbl_7, 'tbl_8': tbl_8, 'tbl_9': tbl_9, 'tbl_10': tbl_10, 'tbl_11': tbl_11, 'tbl_12': tbl_12, 'tbl_13': tbl_13, 'tbl_14': tbl_14, 'tbl_15': tbl_15, 'tbl_16': tbl_16, 'tbl_17': tbl_17, 'tbl_18': tbl_18, 'tbl_19': tbl_19, 'tbl_20': tbl_20, 'tbl_21': tbl_21, 'tbl_22': tbl_22, 'tbl_23': tbl_23, 'tbl_24': tbl_24, 'tbl_25': tbl_25, 'W_top1': W_top1, 'b_top1': b_top1, 'W_top2': W_top2, 'b_top2': b_top2, 'W_top3': W_top3}

def reference(r_dense_features, ids, tbl_0, tbl_1, tbl_2, tbl_3, tbl_4, tbl_5, tbl_6, tbl_7, tbl_8, tbl_9, tbl_10, tbl_11, tbl_12, tbl_13, tbl_14, tbl_15, tbl_16, tbl_17, tbl_18, tbl_19, tbl_20, tbl_21, tbl_22, tbl_23, tbl_24, tbl_25, W_top1, b_top1, W_top2, b_top2, W_top3):
    import jax
    import jax.numpy as jnp

    def _L0_rec_ref(dense_features, sparse_features):
        import jax, jax.numpy as jnp
        import numpy as np
        F = 26
        B, D = dense_features.shape
        combined = jnp.concatenate((dense_features[:, None, :], sparse_features), axis=1)
        interactions = jnp.einsum('bfd,bgd->bfg', combined, combined)
        iu, ju = jnp.triu_indices(F + 1, k=1)
        interactions_flat = interactions[:, iu, ju]
        return jnp.concatenate((dense_features, interactions_flat), axis=1)
    e = jnp.stack([tbl_0[ids[:, 0]], tbl_1[ids[:, 1]], tbl_2[ids[:, 2]], tbl_3[ids[:, 3]], tbl_4[ids[:, 4]], tbl_5[ids[:, 5]], tbl_6[ids[:, 6]], tbl_7[ids[:, 7]], tbl_8[ids[:, 8]], tbl_9[ids[:, 9]], tbl_10[ids[:, 10]], tbl_11[ids[:, 11]], tbl_12[ids[:, 12]], tbl_13[ids[:, 13]], tbl_14[ids[:, 14]], tbl_15[ids[:, 15]], tbl_16[ids[:, 16]], tbl_17[ids[:, 17]], tbl_18[ids[:, 18]], tbl_19[ids[:, 19]], tbl_20[ids[:, 20]], tbl_21[ids[:, 21]], tbl_22[ids[:, 22]], tbl_23[ids[:, 23]], tbl_24[ids[:, 24]], tbl_25[ids[:, 25]]], axis=1)
    z = _L0_rec_ref(r_dense_features, e)
    z = z.reshape(z.shape[0], -1)
    h = jnp.concatenate([z, r_dense_features], axis=1)
    h = jnp.maximum(h @ W_top1 + b_top1, 0.0)
    h = jnp.maximum(h @ W_top2 + b_top2, 0.0)
    y = h @ W_top3
    return y

_drawn_inputs = setup_inputs


def setup_inputs(seed=0):
    import zlib

    import numpy as np

    out = dict(_drawn_inputs(seed))
    spreads = {'b_top1': (0.0, 0.1), 'b_top2': (0.0, 0.1)}
    factors = {}
    for name, (base, spread) in spreads.items():
        noise = np.random.default_rng([zlib.crc32(name.encode()), seed]).standard_normal(out[name].shape)
        drawn = base * np.exp(spread * noise) if base else spread * noise
        out[name] = jnp.asarray(drawn.astype(out[name].dtype))
    for name, factor in factors.items():
        out[name] = (out[name] * factor).astype(out[name].dtype)
    return out
```

```python
from contextlib import ExitStack

import concourse.bass as bass
from concourse import mybir

ACT = mybir.ActivationFunctionType
ALU = mybir.AluOpType
F32 = mybir.dt.float32
I32 = mybir.dt.int32

P = 128
SLOTS = 32
QUADS = P // SLOTS
GROUP = 4
BANK = 512


def dlrm_tower(nc, dense, ids, tables, w_top1, b_top1, w_top2, b_top2, w_top3, out):
    B, D = dense.shape
    NT = len(tables)
    NF = NT + 1
    PAIRS = NF * (NF - 1) // 2
    H1 = w_top1.shape[1]
    H2 = w_top2.shape[1]
    TILES = B // P
    C1, C2 = H1 // P, H2 // P
    COLS = NF - 1
    CHUNKS = (COLS + QUADS - 1) // QUADS
    PER_QUAD = P // QUADS
    PER_BANK = BANK // SLOTS
    GROUPS = [range(1 + i, min(1 + i + GROUP, NF)) for i in range(0, NT, GROUP)]
    NG = len(GROUPS)
    ROWS = C1 + C2 + C2
    assert D == P and w_top1.shape[0] == 2 * D + PAIRS

    with ExitStack() as ctx:
        def sb(name, shape, dt=F32):
            return ctx.enter_context(nc.sbuf_tensor(name, shape, dt))

        def psum(name, shape):
            return ctx.enter_context(nc.psum_tensor(name, shape, F32))

        def sem(name):
            return ctx.enter_context(nc.semaphore(name))

        ident = sb("ident", [P, P])
        ids_sb = sb("ids_sb", [P, TILES, NT], I32)
        dense_sb = sb("dense_sb", [P, TILES, D])
        rows_sb = sb("rows_sb", [ROWS, P])
        cols_sb = sb("cols_sb", [P, ROWS])
        b1_col, b2_col, w3_col = cols_sb[:, 0:C1], cols_sb[:, C1:C1 + C2], cols_sb[:, C1 + C2:ROWS]
        gathered = sb("gathered", [P, TILES, NT, D])
        features_T = sb("features_T", [P, B, SLOTS])
        dense_T = sb("dense_T", [P, B])
        pairs_T = sb("pairs_T", [P, CHUNKS, B])
        w1_pairs = sb("w1_pairs", [P, CHUNKS, H1])
        w1_front = sb("w1_front", [P, H1])
        w1_back = sb("w1_back", [P, H1])
        w1_dense = sb("w1_dense", [P, H1])
        w2_sb = sb("w2_sb", [P, C1, H2])
        h1_T = sb("h1_T", [P, C1, B])
        h2_T = sb("h2_T", [P, C2, B])
        y_sb = sb("y_sb", [1, B])

        turn_ps = psum("turn_ps", [P, 2, GROUP, P])
        dots_ps = psum("dots_ps", [P, PER_QUAD, SLOTS])
        h1_ps = psum("h1_ps", [P, 2, BANK])
        h2_ps = psum("h2_ps", [P, BANK])
        y_ps = psum("y_ps", [1, B])

        s_ids = sem("s_ids")
        s_dense = sem("s_dense")
        s_rows = sem("s_rows")
        s_w1_zeroed = sem("s_w1_zeroed")
        s_w1_pairs = sem("s_w1_pairs")
        s_w1_ends = sem("s_w1_ends")
        s_w1_summed = sem("s_w1_summed")
        s_w2 = sem("s_w2")
        s_ident_zero = sem("s_ident_zero")
        s_ident = sem("s_ident")
        s_pads = sem("s_pads")
        s_gathered = [[sem(f"s_gathered_{t}_{g}") for g in range(NG)] for t in range(TILES)]
        s_turned = sem("s_turned")
        s_moved = [sem("s_moved_act"), sem("s_moved_dve")]
        s_dots = sem("s_dots")
        s_pairs = [sem("s_pairs_act"), sem("s_pairs_dve")]
        s_h1 = sem("s_h1")
        s_h1_relu = sem("s_h1_relu")
        s_h2 = sem("s_h2")
        s_h2_relu = sem("s_h2_relu")
        s_y = sem("s_y")
        s_y_sb = sem("s_y_sb")
        s_out = sem("s_out")

        def turn(t, g):
            return 2 + NG * t + g

        def turns_of(engine, k):
            return (k - engine) // 2 + 1 if k >= engine else 0

        def wait_moved(eng, k):
            for e in range(2):
                eng.wait_ge(s_moved[e], turns_of(e, k))

        block = ctx.enter_context(nc.Block())

        @block.sync
        def _(sp):
            sp.dma_start(ids_sb[:, :, :], ids.rearrange("(t p) f -> p t f", p=P)).then_inc(s_ids, 16)
            sp.dma_start(rows_sb[0:C1, :], b_top1.rearrange("(c p) -> c p", p=P)).then_inc(s_rows, 16)
            sp.dma_start(rows_sb[C1:C1 + C2, :], b_top2.rearrange("(c p) -> c p", p=P)).then_inc(s_rows, 16)
            sp.dma_start(rows_sb[C1 + C2:ROWS, :], w_top3.rearrange("(c p) o -> c (p o)", p=P)).then_inc(s_rows, 16)
            sp.dma_start(dense_sb[:, :, :], dense.rearrange("(t p) d -> p t d", p=P)).then_inc(s_dense, 16)
            sp.dma_start(w1_front[:, :], w_top1[0:D, :]).then_inc(s_w1_ends, 16)
            sp.dma_start(w1_back[:, :], w_top1[D + PAIRS:2 * D + PAIRS, :]).then_inc(s_w1_ends, 16)
            sp.wait_ge(s_w1_zeroed, 1)
            row = D
            for f in range(COLS):
                at = SLOTS * (f % QUADS)
                sp.dma_start(w1_pairs[at + f + 1:at + NF, f // QUADS, :],
                             w_top1[row:row + NF - 1 - f, :]).then_inc(s_w1_pairs, 16)
                row += NF - 1 - f
            sp.dma_start(w2_sb[:, :, :], w_top2.rearrange("(c p) n -> p c n", p=P)).then_inc(s_w2, 16)
            sp.wait_ge(s_y_sb, TILES)
            sp.dma_start(out.rearrange("b o -> o b"), y_sb[:, :]).then_inc(s_out, 16)
            sp.wait_ge(s_out, 16)

        @block.gpsimd
        def _(pool):
            nc.gpsimd.memset(ident[:, :], 0.0).then_inc(s_ident_zero, 1)
            pool.wait_ge(s_ident_zero, 1)
            nc.gpsimd.affine_select(out=ident[:, :], in_=ident[:, :], compare_op=ALU.not_equal, fill=1.0,
                                    base=0, pattern=[[-1, P]], channel_multiplier=1).then_inc(s_ident, 1)
            pool.wait_ge(s_ids, 16)
            for t in range(TILES):
                for g, slots in enumerate(GROUPS):
                    for s in slots:
                        nc.gpsimd.indirect_dma_start(
                            gathered[:, t, s - 1, :], None, tables[s - 1],
                            bass.IndirectOffsetOnAxis(ap=ids_sb[:, t, s - 1:s], axis=0),
                        ).then_inc(s_gathered[t][g], 16)

        def tile_cols(t):
            return slice(t * P, (t + 1) * P)

        def group_view(t, slots):
            return features_T[:, tile_cols(t), slots.start:slots.stop].rearrange("p b s -> p s b")

        def dots_view(j, f0, n):
            return dots_ps[SLOTS * j:SLOTS * (j + 1), :, f0:f0 + QUADS * (n - 1) + 1:QUADS].rearrange("p b f -> p f b")

        def pairs_view(t, j, f0, n):
            b0 = t * P + j * PER_QUAD
            return pairs_T[SLOTS * f0:SLOTS * (f0 + 1), 0:n, b0:b0 + PER_QUAD]

        def chunk_count(f0):
            return len(range(f0, COLS, QUADS))

        @block.scalar
        def _(act):
            def copy(dst, src):
                return nc.scalar.activation(dst, src, ACT.Copy)

            def move_group(t, g):
                k = turn(t, g)
                if k % 2 == 0:
                    act.wait_ge(s_turned, k + 1)
                    n = len(GROUPS[g])
                    copy(group_view(t, GROUPS[g]), turn_ps[:, 0, 0:n, :]).then_inc(s_moved[0], 1)

            def spread_pairs(t):
                act.wait_ge(s_dots, t + 1)
                for j in range(0, 2):
                    for f0 in range(QUADS):
                        n = chunk_count(f0)
                        last = copy(pairs_view(t, j, f0, n), dots_view(j, f0, n))
                last.then_inc(s_pairs[0], 1)

            def relu_h1(t):
                for c in range(C1):
                    act.wait_ge(s_h1, C1 * t + c + 1)
                    nc.scalar.activation(h1_T[:, c, tile_cols(t)], h1_ps[:, c % 2, 0:P], ACT.Relu,
                                         bias=b1_col[:, c:c + 1]).then_inc(s_h1_relu, 1)

            def relu_h2(t):
                act.wait_ge(s_h2, t + 1)
                for c in range(C2):
                    nc.scalar.activation(h2_T[:, c, tile_cols(t)], h2_ps[:, c * P:(c + 1) * P], ACT.Relu,
                                         bias=b2_col[:, c:c + 1]).then_inc(s_h2_relu, 1)

            def move_y(t):
                act.wait_ge(s_y, t + 1)
                copy(y_sb[:, tile_cols(t)], y_ps[:, tile_cols(t)]).then_inc(s_y_sb, 1)

            act.wait_ge(s_turned, 1)
            copy(cols_sb[:, :], turn_ps[:, 0, 0, 0:ROWS]).then_inc(s_moved[0], 1)
            act.wait_ge(s_moved[0], 1)
            for t in range(TILES):
                for g in range(NG):
                    move_group(t, g)
                    if t and g == 0:
                        relu_h1(t - 1)
                    if t and g == 2:
                        relu_h2(t - 1)
                    if t and g == 3:
                        move_y(t - 1)
                spread_pairs(t)
            relu_h1(TILES - 1)
            relu_h2(TILES - 1)
            move_y(TILES - 1)

        @block.vector
        def _(dve):
            nc.vector.memset(w1_pairs[:, :, :], 0.0).then_inc(s_w1_zeroed, 1)
            nc.vector.memset(features_T[:, :, NF:SLOTS], 0.0).then_inc(s_pads, 1)
            for f0 in range(QUADS):
                if chunk_count(f0) < CHUNKS:
                    nc.vector.memset(pairs_T[SLOTS * f0:SLOTS * (f0 + 1), CHUNKS - 1, :], 0.0).then_inc(s_pads, 1)

            def move_group(t, g):
                k = turn(t, g)
                if k % 2 == 1:
                    dve.wait_ge(s_turned, k + 1)
                    n = len(GROUPS[g])
                    nc.vector.tensor_copy(group_view(t, GROUPS[g]), turn_ps[:, 1, 0:n, :]).then_inc(s_moved[1], 1)

            def spread_pairs(t):
                dve.wait_ge(s_dots, t + 1)
                for j in range(2, QUADS):
                    for f0 in range(QUADS):
                        n = chunk_count(f0)
                        last = nc.vector.tensor_copy(pairs_view(t, j, f0, n), dots_view(j, f0, n))
                last.then_inc(s_pairs[1], 1)

            dve.wait_ge(s_turned, 2)
            nc.vector.tensor_copy(dense_T[:, :], turn_ps[:, 1, :, :].rearrange("p t b -> p (t b)"))
            nc.vector.tensor_copy(features_T[:, :, 0], turn_ps[:, 1, :, :].rearrange("p t b -> p (t b)")).then_inc(s_moved[1], 1)
            dve.wait_ge(s_w1_ends, 32)
            nc.vector.tensor_tensor(w1_dense[:, :], w1_front[:, :], w1_back[:, :], ALU.add).then_inc(s_w1_summed, 1)
            for t in range(TILES):
                for g in range(NG):
                    move_group(t, g)
                spread_pairs(t)

        @block.tensor
        def _(pe):
            def turn_group(t, g):
                k = turn(t, g)
                pe.wait_ge(s_gathered[t][g], 16 * len(GROUPS[g]))
                pe.wait_ge(s_moved[k % 2], turns_of(k % 2, k - 2))
                for i, s in enumerate(GROUPS[g]):
                    last = nc.tensor.transpose(turn_ps[:, k % 2, i, :], gathered[:, t, s - 1, :], ident[:, :])
                last.then_inc(s_turned, 1)

            def multiply_pairs(t):
                wait_moved(pe, turn(t, NG - 1))
                if t:
                    pe.wait_ge(s_pairs[0], t)
                    pe.wait_ge(s_pairs[1], t)
                for i in range(PER_QUAD):
                    for j in range(QUADS):
                        x = features_T[:, t * P + j * PER_QUAD + i, :]
                        last = nc.tensor.matmul(dots_ps[SLOTS * j:SLOTS * (j + 1), i, 0:COLS], x, x[:, 0:COLS],
                                                start=True, stop=True)
                last.then_inc(s_dots, 1)

            def layer1(t):
                pe.wait_ge(s_pairs[0], t + 1)
                pe.wait_ge(s_pairs[1], t + 1)
                for c in range(C1):
                    if C1 * t + c >= 2:
                        pe.wait_ge(s_h1_relu, C1 * t + c - 1)
                    out_c = h1_ps[:, c % 2, 0:P]
                    cols = slice(c * P, (c + 1) * P)
                    nc.tensor.matmul(out_c, w1_dense[:, cols], dense_T[:, tile_cols(t)], start=True, stop=False)
                    for q in range(CHUNKS):
                        last = nc.tensor.matmul(out_c, w1_pairs[:, q, cols], pairs_T[:, q, tile_cols(t)],
                                                start=False, stop=(q == CHUNKS - 1))
                    last.then_inc(s_h1, 1)

            def layer2(t):
                pe.wait_ge(s_h1_relu, C1 * (t + 1))
                if t:
                    pe.wait_ge(s_h2_relu, C2 * t)
                for m in range(C2):
                    for c in range(C1):
                        last = nc.tensor.matmul(h2_ps[:, m * P:(m + 1) * P], w2_sb[:, c, m * P:(m + 1) * P], h1_T[:, c, tile_cols(t)],
                                                start=(c == 0), stop=(c == C1 - 1))
                last.then_inc(s_h2, 1)

            def layer3(t):
                pe.wait_ge(s_h2_relu, C2 * (t + 1))
                if t:
                    pe.wait_ge(s_y_sb, t)
                for m in range(C2):
                    last = nc.tensor.matmul(y_ps[:, tile_cols(t)], w3_col[:, m:m + 1], h2_T[:, m, tile_cols(t)],
                                            start=(m == 0), stop=(m == C2 - 1))
                last.then_inc(s_y, 1)

            pe.wait_ge(s_ident, 1)
            pe.wait_ge(s_rows, 48)
            nc.tensor.transpose(turn_ps[:, 0, 0, 0:ROWS], rows_sb[:, :], ident[0:ROWS, 0:ROWS]).then_inc(s_turned, 1)
            pe.wait_ge(s_dense, 16)
            for t in range(TILES):
                last = nc.tensor.transpose(turn_ps[:, 1, t, :], dense_sb[:, t, :], ident[:, :])
            last.then_inc(s_turned, 1)
            for t in range(TILES):
                for g in range(NG):
                    turn_group(t, g)
                    if t and g == 0:
                        if t == 1:
                            pe.wait_ge(s_w1_pairs, 16 * COLS)
                            pe.wait_ge(s_w1_summed, 1)
                        layer1(t - 1)
                    if t and g == 2:
                        if t == 1:
                            pe.wait_ge(s_w2, 16)
                        layer2(t - 1)
                    if t and g == 3:
                        layer3(t - 1)
                if t == 0:
                    pe.wait_ge(s_pads, 1 + sum(chunk_count(f0) < CHUNKS for f0 in range(QUADS)))
                multiply_pairs(t)
            layer1(TILES - 1)
            layer2(TILES - 1)
            layer3(TILES - 1)


_TABLES = [f"tbl_{i}" for i in range(26)]
_WEIGHTS = ["W_top1", "b_top1", "W_top2", "b_top2", "W_top3"]


def kernel(**inputs):
    import numpy as _np
    import concourse.bacc as _bacc
    from concourse import mybir as _mybir
    from concourse.bass_utils import run_bass_kernel_spmd as _run

    nc = _bacc.Bacc("TRN2", target_bir_lowering=False, num_devices=1)
    arrays, aps = {}, {}
    for name in ["r_dense_features", "ids"] + _TABLES + _WEIGHTS:
        a = _np.ascontiguousarray(inputs[name])
        arrays[f"in_{name}_dram"] = a
        aps[name] = nc.dram_tensor(f"in_{name}_dram", a.shape, _mybir.dt.from_np(a.dtype), kind="ExternalInput").ap()
    out = nc.dram_tensor("out_0_dram", (512, 1), _mybir.dt.float32, kind="ExternalOutput").ap()
    dlrm_tower(nc, aps["r_dense_features"], aps["ids"], [aps[n] for n in _TABLES], *[aps[n] for n in _WEIGHTS], out)
    r = _run(nc, [arrays], core_ids=[0])
    return r.results[0]["out_0_dram"]
```

```python
from contextlib import ExitStack

import concourse.bass as bass
from concourse import mybir

ACT = mybir.ActivationFunctionType
ALU = mybir.AluOpType
F32 = mybir.dt.float32
F32R = mybir.dt.float32r
I32 = mybir.dt.int32

P = 128
SLOTS = 32
QUADS = P // SLOTS
BANK = 512
HOT = [9, 13, 18, 19, 20, 25, 26]
GROUPS = [(14, 17, 1), (21, 24, 1), (10, 12, 1), (5, 8, 1), (1, 4, 1)]
EARLY_GROUPS = 3
PARTS = 4


def dlrm_tower(nc, dense, ids, ids_T, tables, w_top1, b_top1, w_top2, b_top2, w_top3, out):
    B, D = dense.shape
    NT = len(tables)
    NF = NT + 1
    PAIRS = NF * (NF - 1) // 2
    H1 = w_top1.shape[1]
    H2 = w_top2.shape[1]
    TILES = B // P
    LAST = TILES - 1
    C1, C2 = H1 // P, H2 // P
    COLS = NF - 1
    CHUNKS = (COLS + QUADS - 1) // QUADS
    WIDE = 3
    PACK = QUADS * WIDE
    packed_rows = {q: NF - 1 - QUADS * q for q in range(WIDE, CHUNKS)}
    packed_cols = {q: min(QUADS, COLS - QUADS * q) for q in range(WIDE, CHUNKS)}
    packed_at = {q: sum(packed_rows[i] * packed_cols[i] for i in range(WIDE, q)) for q in range(WIDE, CHUNKS + 1)}
    PACKED = packed_at[CHUNKS]
    BATCHES = [(t, 1) for t in range(TILES)]
    LAST_BATCH = len(BATCHES) - 1
    PER_QUAD = P // QUADS
    NG = len(GROUPS)
    NHOT = len(HOT)
    ROWS = C1 + C2 + C2
    group_slots = [list(range(a, z + 1, step)) for a, z, step in GROUPS]
    fetched = [s for slots in group_slots for s in slots]
    place = {s: i for i, s in enumerate(fetched)}
    hot_rows = tables[HOT[0] - 1].shape[0]
    FULL = hot_rows // P
    REST = hot_rows - FULL * P
    HC = FULL + 1
    assert D == P and B == BANK and w_top1.shape[0] == 2 * D + PAIRS
    assert all(tables[s - 1].shape[0] == hot_rows for s in HOT) and 0 < REST < P
    assert sorted(HOT + fetched) == list(range(1, NF))
    assert all(s < PACK for slots in group_slots[EARLY_GROUPS:] for s in slots)

    with ExitStack() as ctx:
        def sb(name, shape, dt=F32):
            return ctx.enter_context(nc.sbuf_tensor(name, shape, dt))

        def psum(name, shape):
            return ctx.enter_context(nc.psum_tensor(name, shape, F32))

        def sem(name):
            return ctx.enter_context(nc.semaphore(name))

        spread_dram = nc.dram_tensor("spread_dram", (TILES, CHUNKS - WIDE, P, P), F32, kind="Internal").ap()
        ident = sb("ident", [P, P])
        ids_sb = sb("ids_sb", [P, TILES, NT], I32)
        hot_ids = sb("hot_ids", [P, NHOT, B], I32)
        row_number_int = sb("row_number_int", [P, HC], I32)
        row_number = sb("row_number", [P, HC])
        minus_row = sb("minus_row", [P, 1])
        one_col = sb("one_col", [P, 1])
        table_sb = sb("table_sb", [P, 2, HC, D])
        table_hi = sb("table_hi", [P, 2, HC, D], F32R)
        table_lo = sb("table_lo", [P, 2, HC, D], F32R)
        onehot = sb("onehot", [P, HC, B], F32R)
        dense_sb = sb("dense_sb", [P, TILES, D])
        rows_sb = sb("rows_sb", [ROWS, P])
        cols_sb = sb("cols_sb", [P, ROWS])
        b1_col, b2_col, w3_col = cols_sb[:, 0:C1], cols_sb[:, C1:C1 + C2], cols_sb[:, C1 + C2:ROWS]
        gathered = sb("gathered", [P, TILES, len(fetched), D])
        features_T = sb("features_T", [P, B, SLOTS])
        dense_T = sb("dense_T", [P, B])
        pairs_T = sb("pairs_T", [P, CHUNKS, B])
        packed_T = sb("packed_T", [PACKED, B])
        w1_pairs = sb("w1_pairs", [P, WIDE, H1])
        w1_packed = sb("w1_packed", [PACKED, H1])
        w1_back = sb("w1_back", [P, H1])
        w1_dense = sb("w1_dense", [P, H1])
        w2_sb = sb("w2_sb", [P, C1, H2])
        h1_T = sb("h1_T", [P, C1, B])
        h2_T = sb("h2_T", [P, C2, B])
        y_sb = sb("y_sb", [1, B])

        turn_ps = psum("turn_ps", [P, 2, QUADS, P])
        dots_ps = psum("dots_ps", [P, 2, PER_QUAD * SLOTS])
        mlp_ps = psum("mlp_ps", [P, 2, BANK])
        s_ids = sem("s_ids")
        s_table = [sem(f"s_table_{h}") for h in range(NHOT)]
        s_row_number_int = sem("s_row_number_int")
        s_row_number = sem("s_row_number")
        s_hi = sem("s_hi")
        s_lo = sem("s_lo")
        s_onehot = sem("s_onehot")
        s_distance = sem("s_distance")
        s_onehot_rest = sem("s_onehot_rest")
        s_onehot_used = sem("s_onehot_used")
        s_hot_moved = sem("s_hot_moved")
        s_dense = sem("s_dense")
        s_rows = sem("s_rows")
        s_w1_zeroed = sem("s_w1_zeroed")
        s_w1_pairs = sem("s_w1_pairs")
        s_w1_ends = sem("s_w1_ends")
        s_w1_summed = sem("s_w1_summed")
        s_w2 = sem("s_w2")
        s_ident_zero = sem("s_ident_zero")
        s_ident = sem("s_ident")
        s_pads = sem("s_pads")
        s_gathered = [[sem(f"s_gathered_{t}_{g}") for g in range(NG)] for t in range(TILES)]
        s_turned = sem("s_turned")
        s_moved = sem("s_moved")
        s_dense_moved = sem("s_dense_moved")
        s_dots = sem("s_dots")
        s_pairs = [sem("s_pairs_act"), sem("s_pairs_dve")]
        s_end_zeroed = sem("s_end_zeroed")
        s_spread_out = [sem(f"s_spread_out_{t}") for t in range(TILES)]
        s_packed = [sem(f"s_packed_{b}") for b in range(len(BATCHES))]
        s_h1 = sem("s_h1")
        s_h1_relu = [sem("s_h1_relu_act"), sem("s_h1_relu_dve")]
        s_h2 = sem("s_h2")
        s_h2_relu = [sem("s_h2_relu_act"), sem("s_h2_relu_dve")]
        s_out = sem("s_out")

        def dots_buffer(t):
            return dots_ps[:, min(t, 1), :]

        N_PADS = 1 + NG - EARLY_GROUPS

        def group(t, g):
            return [("group", t, g)]

        def pairs(t, *between):
            steps = []
            for part in range(PARTS):
                steps += [("pairs", t, part)]
                steps += [("spread", t, part // 2)] if part % 2 else []
                steps += group(*between[part]) if part < len(between) else []
            return steps

        def layer1(b, *chunks):
            return [("layer1", b, q) for q in chunks]

        STEPS = [("rows",), ("dense",), ("hot", 0), ("hot", 1)]
        STEPS += group(0, 0) + [("hot", 2)] + group(0, 1) + [("hot", 3)] + group(0, 2) + [("hot", 4)]
        STEPS += group(0, 3) + [("hot", 5)] + group(0, 4) + group(1, 0) + [("hot", 6)] + group(1, 1)
        STEPS += pairs(0, (1, 2), (1, 3)) + group(1, 4) + layer1(0, "dense")
        STEPS += pairs(1, (2, 0)) + layer1(0, *range(WIDE)) + group(2, 1) + layer1(0, "packed")
        STEPS += group(2, 2) + [("layer2", 0)] + layer1(1, "dense", *range(WIDE)) + group(2, 3)
        STEPS += [("layer3", 0)] + layer1(1, "packed") + [("layer2", 1)] + group(2, 4)
        STEPS += layer1(2, "dense") + pairs(2, (3, 0)) + [("layer3", 1)] + group(3, 1)
        STEPS += layer1(2, *range(WIDE)) + group(3, 2)
        STEPS += [("early_pairs",), ("early_spread",)] + layer1(2, "packed") + group(3, 3)
        STEPS += [("layer2", 2)] + layer1(3, "dense") + group(3, 4) + [("layer3", 2)]
        STEPS += [("late_pairs", 0), ("late_spread", 0), ("late_pairs", 1), ("late_spread", 1)]
        STEPS += layer1(3, "packed", *range(WIDE)) + [("layer2", 3), ("layer3", 3)]

        chunks_of = [[step[2] for step in STEPS if step[:2] == ("layer1", b)] for b in range(len(BATCHES))]
        assert all(sorted(map(str, x)) == sorted(map(str, [*range(WIDE), "dense", "packed"])) for x in chunks_of)

        TURNS = [step for step in STEPS if step[0] in ("rows", "dense", "group", "layer3")]

        def turn(*step):
            return TURNS.index(step)

        def moved_halves(t, half=1):
            return 2 * t + half + 1

        EARLY_MOVED = 2 * LAST + 1
        LATE_MOVED = EARLY_MOVED + 2

        def batch_cols(b):
            t, n = BATCHES[b]
            return slice(t * P, (t + n) * P)

        def tile_cols(t):
            return slice(t * P, (t + 1) * P)

        def group_view(t, g):
            a, z, step = GROUPS[g]
            return features_T[:, tile_cols(t), a:z + 1:step].rearrange("p b s -> p s b")

        def hot_parts():
            return [(slice(0, P), slice(0, FULL)), (slice(0, REST), slice(FULL, HC))]

        def chunk_count(f0):
            return len(range(f0, COLS, QUADS))

        def spread(copy, quads, t, view, samples, first_chunk, end_chunk):
            for j in quads:
                for f0 in range(QUADS):
                    n = min(chunk_count(f0), end_chunk) - first_chunk
                    src = view[SLOTS * j:SLOTS * (j + 1), :, f0:f0 + QUADS * (n - 1) + 1:QUADS]
                    b0 = t * P + j * PER_QUAD
                    cols = slice(b0 + samples.start, b0 + samples.stop)
                    last = copy(pairs_T[SLOTS * f0:SLOTS * (f0 + 1), first_chunk:first_chunk + n, cols],
                                src.rearrange("p b f -> p f b"))
            return last

        def half_samples(half):
            return range(half * PER_QUAD // 2, (half + 1) * PER_QUAD // 2)

        def dots_view(t, half):
            return dots_buffer(t)[:, half * BANK:(half + 1) * BANK].rearrange("p (b s) -> p b s", s=SLOTS)

        EARLY = COLS - PACK
        early_ps = dots_buffer(LAST)[:, 0:PER_QUAD * EARLY].rearrange("p (b s) -> p b s", s=EARLY)
        late_ps = [dots_buffer(LAST)[:, at:at + PER_QUAD // 2 * PACK].rearrange("p (b s) -> p b s", s=PACK)
                   for at in (BANK, 0)]
        assert PER_QUAD * EARLY <= BANK

        def wait_spread(eng, n):
            eng.wait_ge(s_pairs[0], n)
            eng.wait_ge(s_pairs[1], n)

        def spread_step(eng, e, copy, step, *a):
            quads = range(2 * e, 2 * e + 2)
            if step == "spread":
                t, half = a
                eng.wait_ge(s_dots, moved_halves(t, half))
                last = spread(copy, quads, t, dots_view(t, half), half_samples(half), 0, CHUNKS)
            elif step == "early_spread":
                eng.wait_ge(s_dots, EARLY_MOVED)
                last = spread(copy, quads, LAST, early_ps, range(PER_QUAD), WIDE, CHUNKS)
            else:
                half, = a
                eng.wait_ge(s_dots, EARLY_MOVED + half + 1)
                last = spread(copy, quads, LAST, late_ps[half], half_samples(half), 0, WIDE)
            last.then_inc(s_pairs[e], 1)

        def h1_relu_count(b, c):
            return C1 // 2 * b + c // 2 + 1

        def h2_sum(b, m):
            return mlp_ps[:, m, 0:BATCHES[b][1] * P]

        def y_sum(b):
            bank = turn_ps[0:1, turn("layer3", b) % 2, :, :].rearrange("p a b -> p (a b)")
            return bank[:, 0:BATCHES[b][1] * P]

        def h1_sum(b, c):
            n = BATCHES[b][1] * P
            if c >= 2:
                return dots_ps[:, 0, (c - 2) * BANK:(c - 2) * BANK + n]
            return mlp_ps[:, c, 0:n]

        block = ctx.enter_context(nc.Block())

        @block.sync
        def _(sp):
            def load_table(h):
                if h >= 2:
                    sp.wait_ge(s_lo, h - 1)
                sp.dma_start(hot_ids[:, h, :], ids_T[HOT[h] - 1, :].partition_broadcast(P)).then_inc(s_table[h], 16)
                table = tables[HOT[h] - 1]
                sp.dma_start(table_sb[:, h % 2, 0:FULL, :],
                             table[0:FULL * P, :].rearrange("(p c) d -> p c d", p=P)).then_inc(s_table[h], 16)
                sp.dma_start(table_sb[0:REST, h % 2, FULL, :], table[FULL * P:hot_rows, :]).then_inc(s_table[h], 16)

            def load_w1_pairs(f):
                row = D + sum(NF - 1 - i for i in range(f))
                q, j = divmod(f, QUADS)
                if f < PACK:
                    dst = w1_pairs[SLOTS * j + f + 1:SLOTS * j + NF, q, :]
                else:
                    end = packed_at[q] + packed_rows[q] * (j + 1)
                    dst = w1_packed[end - (NF - 1 - f):end, :]
                sp.dma_start(dst, w_top1[row:row + NF - 1 - f, :]).then_inc(s_w1_pairs, 16)

            sp.dma_start(ids_sb[:, :, :], ids.rearrange("(t p) f -> p t f", p=P)).then_inc(s_ids, 16)
            load_table(0)
            sp.dma_start(rows_sb[0:C1, :], b_top1.rearrange("(c p) -> c p", p=P)).then_inc(s_rows, 16)
            sp.dma_start(rows_sb[C1:C1 + C2, :], b_top2.rearrange("(c p) -> c p", p=P)).then_inc(s_rows, 16)
            sp.dma_start(rows_sb[C1 + C2:ROWS, :], w_top3.rearrange("(c p) o -> c (p o)", p=P)).then_inc(s_rows, 16)
            sp.dma_start(dense_sb[:, :, :], dense.rearrange("(t p) d -> p t d", p=P)).then_inc(s_dense, 16)
            load_table(1)
            sp.dma_start(w1_dense[:, :], w_top1[0:D, :]).then_inc(s_w1_ends, 16)
            sp.dma_start(w1_back[:, :], w_top1[D + PAIRS:2 * D + PAIRS, :]).then_inc(s_w1_ends, 16)
            sp.dma_start(w2_sb[:, :, :], w_top2.rearrange("(c p) n -> p c n", p=P)).then_inc(s_w2, 16)
            sp.wait_ge(s_w1_zeroed, 2)
            for h in range(2, NHOT):
                load_table(h)
                for f in range((h - 2) * COLS // (NHOT - 2), (h - 1) * COLS // (NHOT - 2)):
                    load_w1_pairs(f)
            for t in range(TILES):
                wait_spread(sp, EARLY_MOVED if t == LAST else moved_halves(t))
                if t == 0:
                    sp.wait_ge(s_end_zeroed, 1)
                sp.dma_start(spread_dram[t].rearrange("q p b -> p q b"),
                             pairs_T[:, WIDE:CHUNKS, tile_cols(t)]).then_inc(s_spread_out[t], 16)
                sp.wait_ge(s_spread_out[t], 16)
                for q in range(WIDE, CHUNKS):
                    chunk = spread_dram[t, q - WIDE].rearrange("(j s) b -> j s b", s=SLOTS)
                    sp.dma_start(packed_T[packed_at[q]:packed_at[q + 1], tile_cols(t)],
                                 chunk[0:packed_cols[q], QUADS * q + 1:NF, :]).then_inc(s_packed[t], 16)
            sp.wait_ge(s_moved, len(TURNS))
            sp.dma_start(out.rearrange("b o -> o b"), y_sb[:, :]).then_inc(s_out, 16)
            sp.wait_ge(s_out, 16)

        @block.gpsimd
        def _(pool):
            nc.gpsimd.memset(ident[:, :], 0.0).then_inc(s_ident_zero, 1)
            nc.gpsimd.iota(row_number_int[:, 0:FULL], pattern=[[1, FULL]], base=0,
                           channel_multiplier=FULL).then_inc(s_row_number_int, 1)
            nc.gpsimd.iota(row_number_int[:, FULL:HC], pattern=[[1, 1]], base=FULL * P,
                           channel_multiplier=1).then_inc(s_row_number_int, 1)
            pool.wait_ge(s_ident_zero, 1)
            nc.gpsimd.affine_select(out=ident[:, :], in_=ident[:, :], compare_op=ALU.not_equal, fill=1.0,
                                    base=0, pattern=[[-1, P]], channel_multiplier=1).then_inc(s_ident, 1)
            pool.wait_ge(s_ids, 16)
            for t in range(TILES):
                for g in range(NG):
                    for s in group_slots[g]:
                        nc.gpsimd.indirect_dma_start(
                            gathered[:, t, place[s], :], None, tables[s - 1],
                            bass.IndirectOffsetOnAxis(ap=ids_sb[:, t, s - 1:s], axis=0),
                        ).then_inc(s_gathered[t][g], 16)

        @block.scalar
        def _(act):
            def copy(dst, src):
                return nc.scalar.activation(dst, src, ACT.Copy)

            def zero(dst):
                src = ident[:, 0:1].to_broadcast([P, dst.shape[1] * dst.shape[2]])
                nc.scalar.activation(dst, src.rearrange("p (a b) -> p a b", b=dst.shape[2]), ACT.Copy,
                                     scale=0.0).then_inc(s_pads, 1)

            def bias_rows():
                act.wait_ge(s_turned, 1)
                copy(cols_sb[:, :], turn_ps[:, 0, 0, 0:ROWS]).then_inc(s_moved, 1)

            def dense_features():
                act.wait_ge(s_dense_moved, 1)
                copy(features_T[:, :, 0], turn_ps[:, 1, :, :].rearrange("p t b -> p (t b)")).then_inc(s_moved, 1)

            def split_table(h):
                act.wait_ge(s_table[h], 48)
                if h >= 2:
                    act.wait_ge(s_onehot_used, HC * (h - 1))
                for rows, chunks in hot_parts():
                    copy(table_hi[rows, h % 2, chunks, :], table_sb[rows, h % 2, chunks, :]).then_inc(s_hi, 1)

            def move_hot(h):
                act.wait_ge(s_onehot_used, HC * (h + 1))
                copy(features_T[:, :, HOT[h]], mlp_ps[:, h % 2, :]).then_inc(s_hot_moved, 1)

            def move_group(t, g):
                k = turn("group", t, g)
                act.wait_ge(s_turned, k + 1)
                if t == LAST and g == EARLY_GROUPS:
                    act.wait_ge(s_dots, EARLY_MOVED)
                copy(group_view(t, g), turn_ps[:, k % 2, 0:len(group_slots[g]), :]).then_inc(s_moved, 1)

            def relu_h1(b, c):
                act.wait_ge(s_h1, C1 * b + c + 1)
                nc.scalar.activation(h1_T[:, c, batch_cols(b)], h1_sum(b, c), ACT.Relu,
                                     bias=b1_col[:, c:c + 1]).then_inc(s_h1_relu[0], 1)

            def relu_h2(b):
                act.wait_ge(s_h2, C2 * b + 1)
                nc.scalar.activation(h2_T[:, 0, batch_cols(b)], h2_sum(b, 0), ACT.Relu,
                                     bias=b2_col[:, 0:1]).then_inc(s_h2_relu[0], 1)

            def move_y(b):
                k = turn("layer3", b)
                act.wait_ge(s_turned, k + 1)
                copy(y_sb[:, batch_cols(b)], y_sum(b)).then_inc(s_moved, 1)

            def one_hot_rest(h):
                if h >= 1:
                    act.wait_ge(s_onehot_used, HC * h)
                x = onehot[0:REST, FULL, :]
                nc.scalar.activation(x, hot_ids[0:REST, h, :], ACT.Abs,
                                     bias=minus_row[0:REST, :]).then_inc(s_distance, 1)
                act.wait_ge(s_distance, h + 1)
                nc.scalar.activation(x, x.bitcast(F32), ACT.Relu, bias=one_col[0:REST, :],
                                     scale=-1.0).then_inc(s_onehot_rest, 1)

            act.wait_ge(s_ident, 1)
            zero(features_T[:, :, NF:SLOTS])
            for step, *a in STEPS:
                if step == "rows":
                    bias_rows()
                elif step == "dense":
                    split_table(0)
                    act.wait_ge(s_row_number, 3)
                    one_hot_rest(0)
                    dense_features()
                    act.wait_ge(s_moved, 1)
                    split_table(1)
                elif step == "hot":
                    if a[0] + 2 < NHOT:
                        split_table(a[0] + 2)
                    if a[0] + 1 < NHOT:
                        one_hot_rest(a[0] + 1)
                    move_hot(a[0])
                    if a[0] in range(2, 2 + NG - EARLY_GROUPS):
                        zero(group_view(LAST, EARLY_GROUPS + a[0] - 2))
                elif step == "group":
                    move_group(*a)
                elif step in ("spread", "early_spread", "late_spread"):
                    spread_step(act, 0, copy, step, *a)
                elif step == "layer1" and a[1] == chunks_of[a[0]][-1]:
                    for c in range(0, C1, 2):
                        relu_h1(a[0], c)
                elif step == "layer2":
                    relu_h2(*a)
                elif step == "layer3":
                    move_y(*a)

        @block.vector
        def _(dve):
            copy = nc.vector.tensor_copy

            def one_hot(h):
                dve.wait_ge(s_table[h], 48)
                for c in range(FULL):
                    if h:
                        dve.wait_ge(s_onehot_used, HC * (h - 1) + c + 1)
                    nc.vector.tensor_scalar(onehot[:, c, :], hot_ids[:, h, :], row_number[:, c:c + 1], None,
                                            ALU.is_equal).then_inc(s_onehot, 1)

            def low_part(h):
                dve.wait_ge(s_hi, 2 * h + 2)
                for rows, chunks in hot_parts():
                    last = nc.vector.tensor_tensor(table_lo[rows, h % 2, chunks, :], table_sb[rows, h % 2, chunks, :],
                                                   table_hi[rows, h % 2, chunks, :].bitcast(F32), ALU.subtract)
                last.then_inc(s_lo, 1)

            def relu(dst, src, bias):
                return nc.vector.tensor_scalar(dst, src, bias, 0.0, ALU.add, ALU.max)

            def relu_h1(b, c):
                dve.wait_ge(s_h1, C1 * b + c + 1)
                relu(h1_T[:, c, batch_cols(b)], h1_sum(b, c), b1_col[:, c:c + 1]).then_inc(s_h1_relu[1], 1)

            def relu_h2(b):
                dve.wait_ge(s_h2, C2 * b + 2)
                relu(h2_T[:, 1, batch_cols(b)], h2_sum(b, 1), b2_col[:, 1:2]).then_inc(s_h2_relu[1], 1)

            dve.wait_ge(s_row_number_int, 2)
            copy(row_number[:, :], row_number_int[:, :]).then_inc(s_row_number, 1)
            nc.vector.tensor_scalar(minus_row[:, :], row_number_int[:, FULL:HC], -1.0, None,
                                    ALU.mult).then_inc(s_row_number, 1)
            nc.vector.memset(one_col[:, :], 1.0).then_inc(s_row_number, 1)
            nc.vector.memset(w1_pairs[:, :, :], 0.0).then_inc(s_w1_zeroed, 1)
            nc.vector.memset(w1_packed[:, :], 0.0).then_inc(s_w1_zeroed, 1)
            nc.vector.memset(pairs_T[SLOTS * (COLS % QUADS):P, CHUNKS - 1, :], 0.0).then_inc(s_end_zeroed, 1)
            dve.wait_ge(s_row_number, 1)
            low_part(0)
            one_hot(0)
            for step, *a in STEPS:
                if step == "dense":
                    dve.wait_ge(s_turned, 2)
                    dve.wait_ge(s_moved, 1)
                    copy(dense_T[:, :], turn_ps[:, 1, :, :].rearrange("p t b -> p (t b)")).then_inc(s_dense_moved, 1)
                elif step == "hot":
                    if a[0] + 1 < NHOT:
                        low_part(a[0] + 1)
                        one_hot(a[0] + 1)
                    if a[0] == NHOT - 1:
                        dve.wait_ge(s_w1_ends, 32)
                        nc.vector.tensor_tensor(w1_dense[:, :], w1_dense[:, :], w1_back[:, :],
                                                ALU.add).then_inc(s_w1_summed, 1)
                elif step in ("spread", "early_spread", "late_spread"):
                    spread_step(dve, 1, copy, step, *a)
                elif step == "layer1" and a[1] == chunks_of[a[0]][-1]:
                    for c in range(1, C1, 2):
                        relu_h1(a[0], c)
                elif step == "layer2":
                    relu_h2(*a)

        @block.tensor
        def _(pe):
            def bias_rows():
                pe.wait_ge(s_ident, 1)
                pe.wait_ge(s_rows, 48)
                nc.tensor.transpose(turn_ps[:, 0, 0, 0:ROWS], rows_sb[:, :], ident[0:ROWS, 0:ROWS]).then_inc(s_turned, 1)

            def dense_features():
                pe.wait_ge(s_dense, 16)
                for t in range(TILES):
                    last = nc.tensor.transpose(turn_ps[:, 1, t, :], dense_sb[:, t, :], ident[:, :])
                last.then_inc(s_turned, 1)

            def look_up(h):
                pe.wait_ge(s_lo, h + 1)
                if h >= 2:
                    pe.wait_ge(s_hot_moved, h - 1)
                for c in range(HC):
                    rows = P if c < FULL else REST
                    if c < FULL:
                        pe.wait_ge(s_onehot, FULL * h + c + 1)
                    else:
                        pe.wait_ge(s_onehot_rest, h + 1)
                    for i, part in enumerate((table_hi, table_lo)):
                        last = nc.tensor.matmul(mlp_ps[:, h % 2, :], part[0:rows, h % 2, c, :], onehot[0:rows, c, :],
                                                start=(c == 0 and i == 0), stop=(c == HC - 1 and i == 1))
                    last.then_inc(s_onehot_used, 1)

            def turn_group(t, g):
                k = turn("group", t, g)
                pe.wait_ge(s_gathered[t][g], 16 * len(group_slots[g]))
                pe.wait_ge(s_moved, k - 1)
                for i, s in enumerate(group_slots[g]):
                    last = nc.tensor.transpose(turn_ps[:, k % 2, i, :], gathered[:, t, place[s], :], ident[:, :])
                last.then_inc(s_turned, 1)

            def multiply_pairs(t, view, first_col, end_col, sample0, places):
                for n, i in enumerate(places):
                    for j in range(QUADS):
                        x = features_T[:, t * P + j * PER_QUAD + sample0 + n, :]
                        last = nc.tensor.matmul(view[SLOTS * j:SLOTS * (j + 1), i, 0:end_col - first_col], x,
                                                x[:, first_col:end_col], start=True, stop=True)
                return last

            def wait_h1_relu(b, c):
                pe.wait_ge(s_h1_relu[c % 2], h1_relu_count(b, c))

            def wait_h1_bank(b, c):
                if c < C2:
                    if b:
                        pe.wait_ge(s_h2_relu[c], b)
                elif b == 0:
                    wait_spread(pe, moved_halves(0, c - C2))
                else:
                    wait_h1_relu(b - 1, c)

            def layer1(b, q):
                first, final = q == chunks_of[b][0], q == chunks_of[b][-1]
                if b == 0 and q == "dense":
                    pe.wait_ge(s_w1_summed, 1)
                if b == 0 and q == 0:
                    pe.wait_ge(s_w1_pairs, 16 * COLS)
                if q == 0:
                    wait_spread(pe, LATE_MOVED if b == LAST_BATCH else moved_halves(sum(BATCHES[b]) - 1))
                if q == "packed":
                    pe.wait_ge(s_packed[b], 16 * (CHUNKS - WIDE))
                for c in [*range(C2, C1), *range(C2)] if first and b else range(C1):
                    if first:
                        wait_h1_bank(b, c)
                    if q == "dense":
                        w, x = w1_dense, dense_T
                    elif q == "packed":
                        w, x = w1_packed, packed_T
                    else:
                        w, x = w1_pairs[:, q, :], pairs_T[:, q, :]
                    last = nc.tensor.matmul(h1_sum(b, c), w[:, c * P:(c + 1) * P], x[:, batch_cols(b)],
                                            start=first, stop=final)
                    if final:
                        last.then_inc(s_h1, 1)

            def layer2(b):
                if b == 0:
                    pe.wait_ge(s_w2, 16)
                for m in range(C2):
                    for c in range(C1):
                        if m == 0:
                            wait_h1_relu(b, c)
                        last = nc.tensor.matmul(h2_sum(b, m), w2_sb[:, c, m * P:(m + 1) * P], h1_T[:, c, batch_cols(b)],
                                                start=(c == 0), stop=(c == C1 - 1))
                    last.then_inc(s_h2, 1)

            def layer3(b):
                pe.wait_ge(s_moved, turn("layer3", b) - 1)
                for m in range(C2):
                    pe.wait_ge(s_h2_relu[m], b + 1)
                    last = nc.tensor.matmul(y_sum(b), w3_col[:, m:m + 1], h2_T[:, m, batch_cols(b)],
                                            start=(m == 0), stop=(m == C2 - 1))
                last.then_inc(s_turned, 1)

            for step, *a in STEPS:
                if step == "rows":
                    bias_rows()
                elif step == "dense":
                    dense_features()
                elif step == "hot":
                    look_up(*a)
                elif step == "group":
                    turn_group(*a)
                elif step == "pairs":
                    t, part = a
                    if t == 0 and part == 0:
                        pe.wait_ge(s_pads, N_PADS)
                        pe.wait_ge(s_hot_moved, NHOT)
                    if part == 0:
                        pe.wait_ge(s_moved, turn("group", t, NG - 1) + 1)
                    if t == 2 and part % 2 == 0:
                        wait_spread(pe, moved_halves(1, part // 2))
                    n = PER_QUAD // PARTS
                    i0 = n * (part % 2)
                    last = multiply_pairs(t, dots_view(t, part // 2), 0, COLS, n * part, range(i0, i0 + n))
                    if part % 2:
                        last.then_inc(s_dots, 1)
                elif step == "early_pairs":
                    pe.wait_ge(s_moved, turn("group", LAST, EARLY_GROUPS - 1) + 1)
                    wait_spread(pe, moved_halves(LAST - 1, 0))
                    multiply_pairs(LAST, early_ps, PACK, COLS, 0, range(PER_QUAD)).then_inc(s_dots, 1)
                elif step == "late_pairs":
                    half, = a
                    if half == 0:
                        pe.wait_ge(s_moved, turn("group", LAST, NG - 1) + 1)
                        wait_spread(pe, moved_halves(LAST - 1, 1))
                    else:
                        wait_spread(pe, EARLY_MOVED)
                    n = PER_QUAD // 2
                    multiply_pairs(LAST, late_ps[half], 0, PACK, n * half, range(n)).then_inc(s_dots, 1)
                elif step == "layer1":
                    layer1(*a)
                elif step == "layer2":
                    layer2(*a)
                elif step == "layer3":
                    layer3(*a)


_TABLES = [f"tbl_{i}" for i in range(26)]
_WEIGHTS = ["W_top1", "b_top1", "W_top2", "b_top2", "W_top3"]


def kernel(**inputs):
    import numpy as _np
    import concourse.bacc as _bacc
    from concourse import mybir as _mybir
    from concourse.bass_utils import run_bass_kernel_spmd as _run

    nc = _bacc.Bacc("TRN2", target_bir_lowering=False, num_devices=1)
    arrays, aps = {}, {}
    for name in ["r_dense_features", "ids"] + _TABLES + _WEIGHTS:
        a = _np.ascontiguousarray(inputs[name])
        arrays[f"in_{name}_dram"] = a
        aps[name] = nc.dram_tensor(f"in_{name}_dram", a.shape, _mybir.dt.from_np(a.dtype), kind="ExternalInput").ap()
    ids_T = _np.ascontiguousarray(inputs["ids"].T)
    arrays["in_ids_T_dram"] = ids_T
    aps["ids_T"] = nc.dram_tensor("in_ids_T_dram", ids_T.shape, _mybir.dt.from_np(ids_T.dtype), kind="ExternalInput").ap()
    out = nc.dram_tensor("out_0_dram", (512, 1), _mybir.dt.float32, kind="ExternalOutput").ap()
    dlrm_tower(nc, aps["r_dense_features"], aps["ids"], aps["ids_T"], [aps[n] for n in _TABLES], *[aps[n] for n in _WEIGHTS], out)
    r = _run(nc, [arrays], core_ids=[0])
    return r.results[0]["out_0_dram"]
```

```python
from contextlib import ExitStack

import concourse.bass as bass
from concourse import mybir

ACT = mybir.ActivationFunctionType
ALU = mybir.AluOpType
F32 = mybir.dt.float32
F32R = mybir.dt.float32r
I32 = mybir.dt.int32

P = 128
SLOTS = 32
QUADS = P // SLOTS
BANK = 512
HOT = [2, 9, 13, 18, 19, 20, 25, 26]
GROUPS = [(14, 17, 1), (21, 24, 1), (10, 12, 1), (4, 8, 2), (1, 7, 2)]
EARLY_GROUPS = 3
PARTS = 4


def dlrm_tower(nc, dense, ids, ids_T, tables, w_top1, b_top1, w_top2, b_top2, w_top3, out):
    B, D = dense.shape
    NT = len(tables)
    NF = NT + 1
    PAIRS = NF * (NF - 1) // 2
    H1 = w_top1.shape[1]
    H2 = w_top2.shape[1]
    TILES = B // P
    LAST = TILES - 1
    C1, C2 = H1 // P, H2 // P
    COLS = NF - 1
    CHUNKS = (COLS + QUADS - 1) // QUADS
    WIDE = 3
    PACK = QUADS * WIDE
    packed_rows = {q: NF - 1 - QUADS * q for q in range(WIDE, CHUNKS)}
    packed_cols = {q: min(QUADS, COLS - QUADS * q) for q in range(WIDE, CHUNKS)}
    packed_at = {q: sum(packed_rows[i] * packed_cols[i] for i in range(WIDE, q)) for q in range(WIDE, CHUNKS + 1)}
    PACKED = packed_at[CHUNKS]
    PER_QUAD = P // QUADS
    NG = len(GROUPS)
    NHOT = len(HOT)
    ROWS = C1 + C2 + C2
    group_slots = [list(range(a, z + 1, step)) for a, z, step in GROUPS]
    fetched = [s for slots in group_slots for s in slots]
    place = {s: i for i, s in enumerate(fetched)}
    hot_rows = tables[HOT[0] - 1].shape[0]
    HC = -(-hot_rows // P)
    HP = hot_rows // HC
    TAIL = HC - 1
    assert D == P and B == BANK and w_top1.shape[0] == 2 * D + PAIRS
    assert all(tables[s - 1].shape[0] == hot_rows == HC * HP for s in HOT)
    assert sorted(HOT + fetched) == list(range(1, NF))
    assert all(s < PACK for slots in group_slots[EARLY_GROUPS:] for s in slots)

    with ExitStack() as ctx:
        def sb(name, shape, dt=F32):
            return ctx.enter_context(nc.sbuf_tensor(name, shape, dt))

        def psum(name, shape):
            return ctx.enter_context(nc.psum_tensor(name, shape, F32))

        def sem(name):
            return ctx.enter_context(nc.semaphore(name))

        spread_dram = nc.dram_tensor("spread_dram", (TILES, CHUNKS - WIDE, P, P), F32, kind="Internal").ap()
        ident = sb("ident", [P, P])
        ids_sb = sb("ids_sb", [P, TILES, NT], I32)
        hot_ids = sb("hot_ids", [HP, NHOT, B], I32)
        row_number_int = sb("row_number_int", [HP, HC], I32)
        row_number = sb("row_number", [HP, HC])
        minus_row = sb("minus_row", [HP, 1])
        one_col = sb("one_col", [HP, 1])
        table_sb = sb("table_sb", [HP, 2, HC, D])
        table_hi = sb("table_hi", [HP, 2, HC, D], F32R)
        table_lo = sb("table_lo", [HP, 2, HC, D], F32R)
        onehot = sb("onehot", [HP, HC, B], F32R)
        dense_sb = sb("dense_sb", [P, TILES, D])
        rows_sb = sb("rows_sb", [ROWS, P])
        cols_sb = sb("cols_sb", [P, ROWS])
        b1_col, b2_col, w3_col = cols_sb[:, 0:C1], cols_sb[:, C1:C1 + C2], cols_sb[:, C1 + C2:ROWS]
        gathered = sb("gathered", [P, TILES, len(fetched), D])
        features_T = sb("features_T", [P, B, SLOTS])
        dense_T = sb("dense_T", [P, B])
        pairs_T = sb("pairs_T", [P, CHUNKS, B])
        packed_T = sb("packed_T", [PACKED, B])
        w1_pairs = sb("w1_pairs", [P, WIDE, H1])
        w1_packed = sb("w1_packed", [PACKED, H1])
        w1_back = sb("w1_back", [P, H1])
        w1_dense = sb("w1_dense", [P, H1])
        w2_sb = sb("w2_sb", [P, C1, H2])
        h1_T = sb("h1_T", [P, C1, B])
        h2_T = sb("h2_T", [P, C2, B])
        y_sb = sb("y_sb", [1, B])

        turn_ps = psum("turn_ps", [P, 2, QUADS, P])
        dots_ps = psum("dots_ps", [P, 2, PER_QUAD * SLOTS])
        mlp_ps = psum("mlp_ps", [P, 2, BANK])

        s_ids = sem("s_ids")
        s_hot_ids = [sem(f"s_hot_ids_{h}") for h in range(NHOT)]
        s_table = [sem(f"s_table_{h}") for h in range(NHOT)]
        s_dense = sem("s_dense")
        s_rows = sem("s_rows")
        s_w1_pairs = sem("s_w1_pairs")
        s_w1_ends = sem("s_w1_ends")
        s_w2 = sem("s_w2")
        s_gathered = [[sem(f"s_gathered_{t}_{g}") for g in range(NG)] for t in range(TILES)]
        s_ident_zero = sem("s_ident_zero")
        s_ident = sem("s_ident")
        s_row_number_int = sem("s_row_number_int")
        s_row_number = sem("s_row_number")
        s_w1_zeroed = sem("s_w1_zeroed")
        s_end_zeroed = sem("s_end_zeroed")
        s_pads = sem("s_pads")
        s_w1_summed = sem("s_w1_summed")
        s_hi = sem("s_hi")
        s_lo = sem("s_lo")
        s_onehot = sem("s_onehot")
        s_distance = sem("s_distance")
        s_onehot_tail = sem("s_onehot_tail")
        s_onehot_used = sem("s_onehot_used")
        s_hot_moved = sem("s_hot_moved")
        s_turned = sem("s_turned")
        s_moved = sem("s_moved")
        s_dots = sem("s_dots")
        s_pairs = [sem("s_pairs_act"), sem("s_pairs_dve")]
        s_spread_out = [sem(f"s_spread_out_{t}") for t in range(TILES)]
        s_packed = [sem(f"s_packed_{t}") for t in range(TILES)]
        s_h1 = sem("s_h1")
        s_h1_relu = [sem("s_h1_relu_act"), sem("s_h1_relu_dve")]
        s_h2 = sem("s_h2")
        s_h2_relu = [sem("s_h2_relu_act"), sem("s_h2_relu_dve")]
        s_out = sem("s_out")

        N_PADS = 1 + NG - EARLY_GROUPS

        def group(t, g):
            return [("group", t, g)]

        EARLY, LATE = LAST, LAST + 1
        pass_chunks = {EARLY: range(WIDE, CHUNKS), LATE: range(WIDE)}

        def pairs(p, *between):
            steps = []
            for part in range(PARTS):
                steps += [("pairs", p, part)]
                steps += [("spread", p, part // 2)] if part % 2 else []
                steps += between[part] if part < len(between) else []
            return steps

        def layer1(t, *chunks):
            return [("layer1", t, q) for q in chunks]

        STEPS = [("rows",), ("hot", 0), ("dense",), ("hot", 1)]
        STEPS += group(0, 0) + [("hot", 2)] + group(0, 1) + [("hot", 3)] + group(0, 2) + [("hot", 4)]
        STEPS += group(0, 3) + [("hot", 5)] + group(0, 4) + group(1, 0) + [("hot", 6)]
        STEPS += [("hot", 7)] + group(1, 1) + group(1, 2)
        STEPS += pairs(0, group(1, 3), [], group(1, 4))
        STEPS += pairs(1, layer1(0, "dense"), group(2, 0)) + layer1(0, *range(WIDE)) + group(2, 1)
        STEPS += layer1(0, "packed") + group(2, 2) + [("layer2", 0)] + layer1(1, "dense", *range(WIDE)) + group(2, 3)
        STEPS += [("layer3", 0)] + layer1(1, "packed") + group(2, 4) + [("layer2", 1)]
        STEPS += pairs(2, group(3, 0)) + [("layer3", 1)] + layer1(2, "dense") + group(3, 1)
        STEPS += layer1(2, 0) + group(3, 2) + layer1(2, 1)
        STEPS += pairs(EARLY, [], layer1(2, 2)) + layer1(2, "packed") + group(3, 3)
        STEPS += group(3, 4) + [("layer2", 2)]
        STEPS += pairs(LATE, [], layer1(3, "dense")) + [("layer3", 2)]
        STEPS += layer1(3, "packed", *range(WIDE)) + [("layer2", 3), ("layer3", 3)]

        chunks_of = [[step[2] for step in STEPS if step[:2] == ("layer1", t)] for t in range(TILES)]
        assert all(sorted(map(str, x)) == sorted(map(str, [*range(WIDE), "dense", "packed"])) for x in chunks_of)

        TURNS = [step for step in STEPS if step[0] in ("rows", "dense", "group", "layer3")]

        def turn(*step):
            return TURNS.index(step)

        def moved_halves(p, half=1):
            return 2 * p + half + 1

        def tile_cols(t):
            return slice(t * P, (t + 1) * P)

        def group_view(t, g):
            a, z, step = GROUPS[g]
            return features_T[:, tile_cols(t), a:z + 1:step].rearrange("p b s -> p s b")

        def chunk_count(f0):
            return len(range(f0, COLS, QUADS))

        def dots_view(p, half):
            return dots_ps[:, min(p, 1), half * BANK:(half + 1) * BANK].rearrange("p (b s) -> p b s", s=SLOTS)

        def wait_spread(eng, n):
            eng.wait_ge(s_pairs[0], n)
            eng.wait_ge(s_pairs[1], n)

        def spread(eng, e, copy, p, half):
            eng.wait_ge(s_dots, moved_halves(p, half))
            chunks = pass_chunks.get(p, range(CHUNKS))
            n_samples = PER_QUAD // 2
            for j in range(2 * e, 2 * e + 2):
                for f0 in range(QUADS):
                    end = min(chunk_count(f0), chunks.stop)
                    src = dots_view(p, half)[SLOTS * j:SLOTS * (j + 1), :, QUADS * chunks.start + f0:QUADS * (end - 1) + f0 + 1:QUADS]
                    b0 = min(p, LAST) * P + j * PER_QUAD + half * n_samples
                    last = copy(pairs_T[SLOTS * f0:SLOTS * (f0 + 1), chunks.start:end, b0:b0 + n_samples],
                                src.rearrange("p b f -> p f b"))
            last.then_inc(s_pairs[e], 1)

        def h1_relu_count(t, c):
            return C1 // 2 * t + c // 2 + 1

        def h2_sum(m):
            return mlp_ps[:, m, 0:P]

        def y_sum(t):
            return turn_ps[0:1, turn("layer3", t) % 2, 0, :]

        def h1_sum(c):
            if c >= C2:
                return dots_ps[:, 0, (c - C2) * BANK:(c - C2) * BANK + P]
            return mlp_ps[:, c, 0:P]

        block = ctx.enter_context(nc.Block())

        @block.sync
        def _(sp):
            def load_table(h):
                sp.dma_start(hot_ids[:, h, :], ids_T[HOT[h] - 1, :].partition_broadcast(HP)).then_inc(s_hot_ids[h], 16)
                if h >= 2:
                    sp.wait_ge(s_lo, h - 1)
                sp.dma_start(table_sb[:, h % 2, :, :],
                             tables[HOT[h] - 1].rearrange("(p c) d -> p c d", c=HC)).then_inc(s_table[h], 16)

            def load_w1_pairs(f):
                row = D + sum(NF - 1 - i for i in range(f))
                q, j = divmod(f, QUADS)
                if f < PACK:
                    dst = w1_pairs[SLOTS * j + f + 1:SLOTS * j + NF, q, :]
                else:
                    end = packed_at[q] + packed_rows[q] * (j + 1)
                    dst = w1_packed[end - (NF - 1 - f):end, :]
                sp.dma_start(dst, w_top1[row:row + NF - 1 - f, :]).then_inc(s_w1_pairs, 16)

            sp.dma_start(ids_sb[:, :, :], ids.rearrange("(t p) f -> p t f", p=P)).then_inc(s_ids, 16)
            load_table(0)
            sp.dma_start(rows_sb[0:C1, :], b_top1.rearrange("(c p) -> c p", p=P)).then_inc(s_rows, 16)
            sp.dma_start(rows_sb[C1:C1 + C2, :], b_top2.rearrange("(c p) -> c p", p=P)).then_inc(s_rows, 16)
            sp.dma_start(rows_sb[C1 + C2:ROWS, :], w_top3.rearrange("(c p) o -> c (p o)", p=P)).then_inc(s_rows, 16)
            sp.dma_start(dense_sb[:, :, :], dense.rearrange("(t p) d -> p t d", p=P)).then_inc(s_dense, 16)
            load_table(1)
            load_table(2)
            sp.dma_start(w1_dense[:, :], w_top1[0:D, :]).then_inc(s_w1_ends, 16)
            sp.dma_start(w1_back[:, :], w_top1[D + PAIRS:2 * D + PAIRS, :]).then_inc(s_w1_ends, 16)
            sp.dma_start(w2_sb[:, :, :], w_top2.rearrange("(c p) n -> p c n", p=P)).then_inc(s_w2, 16)
            sp.wait_ge(s_w1_zeroed, 2)
            for h in range(3, NHOT):
                load_table(h)
                for f in range((h - 3) * COLS // (NHOT - 3), (h - 2) * COLS // (NHOT - 3)):
                    load_w1_pairs(f)
            for t in range(TILES):
                wait_spread(sp, moved_halves(t))
                if t == 0:
                    sp.wait_ge(s_end_zeroed, 1)
                sp.dma_start(spread_dram[t].rearrange("q p b -> p q b"),
                             pairs_T[:, WIDE:CHUNKS, tile_cols(t)]).then_inc(s_spread_out[t], 16)
                sp.wait_ge(s_spread_out[t], 16)
                for q in range(WIDE, CHUNKS):
                    chunk = spread_dram[t, q - WIDE].rearrange("(j s) b -> j s b", s=SLOTS)
                    sp.dma_start(packed_T[packed_at[q]:packed_at[q + 1], tile_cols(t)],
                                 chunk[0:packed_cols[q], QUADS * q + 1:NF, :]).then_inc(s_packed[t], 16)
            sp.wait_ge(s_moved, len(TURNS))
            sp.dma_start(out.rearrange("b o -> o b"), y_sb[:, :]).then_inc(s_out, 16)
            sp.wait_ge(s_out, 16)

        @block.gpsimd
        def _(pool):
            nc.gpsimd.memset(ident[:, :], 0.0).then_inc(s_ident_zero, 1)
            nc.gpsimd.iota(row_number_int[:, :], pattern=[[1, HC]], base=0,
                           channel_multiplier=HC).then_inc(s_row_number_int, 1)
            pool.wait_ge(s_ident_zero, 1)
            nc.gpsimd.affine_select(out=ident[:, :], in_=ident[:, :], compare_op=ALU.not_equal, fill=1.0,
                                    base=0, pattern=[[-1, P]], channel_multiplier=1).then_inc(s_ident, 1)
            pool.wait_ge(s_ids, 16)
            for t in range(TILES):
                for g in range(NG):
                    for s in group_slots[g]:
                        nc.gpsimd.indirect_dma_start(
                            gathered[:, t, place[s], :], None, tables[s - 1],
                            bass.IndirectOffsetOnAxis(ap=ids_sb[:, t, s - 1:s], axis=0),
                        ).then_inc(s_gathered[t][g], 16)

        @block.scalar
        def _(act):
            def copy(dst, src):
                return nc.scalar.activation(dst, src, ACT.Copy)

            def zero(dst):
                src = ident[:, 0:1].to_broadcast([P, dst.shape[1] * dst.shape[2]])
                nc.scalar.activation(dst, src.rearrange("p (a b) -> p a b", b=dst.shape[2]), ACT.Copy,
                                     scale=0.0).then_inc(s_pads, 1)

            def bias_rows():
                act.wait_ge(s_turned, 1)
                copy(cols_sb[:, :], turn_ps[:, 0, 0, 0:ROWS]).then_inc(s_moved, 1)

            def dense_features():
                act.wait_ge(s_turned, turn("dense") + 1)
                src = turn_ps[:, turn("dense") % 2, :, :].rearrange("p t b -> p (t b)")
                copy(features_T[:, :, 0], src)
                copy(dense_T[:, :], src).then_inc(s_moved, 1)

            def split_table(h):
                act.wait_ge(s_table[h], 16)
                if h >= 2:
                    act.wait_ge(s_onehot_used, HC * (h - 1))
                copy(table_hi[:, h % 2, :, :], table_sb[:, h % 2, :, :]).then_inc(s_hi, 1)

            def move_hot(h):
                act.wait_ge(s_onehot_used, HC * (h + 1))
                copy(features_T[:, :, HOT[h]], mlp_ps[:, h % 2, :]).then_inc(s_hot_moved, 1)

            def move_group(t, g):
                k = turn("group", t, g)
                act.wait_ge(s_turned, k + 1)
                if t == LAST and g == EARLY_GROUPS:
                    act.wait_ge(s_dots, moved_halves(EARLY))
                copy(group_view(t, g), turn_ps[:, k % 2, 0:len(group_slots[g]), :]).then_inc(s_moved, 1)

            def relu_h1(t, c):
                act.wait_ge(s_h1, C1 * t + c + 1)
                nc.scalar.activation(h1_T[:, c, tile_cols(t)], h1_sum(c), ACT.Relu,
                                     bias=b1_col[:, c:c + 1]).then_inc(s_h1_relu[0], 1)

            def relu_h2(t):
                act.wait_ge(s_h2, C2 * t + 1)
                nc.scalar.activation(h2_T[:, 0, tile_cols(t)], h2_sum(0), ACT.Relu,
                                     bias=b2_col[:, 0:1]).then_inc(s_h2_relu[0], 1)

            def move_y(t):
                k = turn("layer3", t)
                act.wait_ge(s_turned, k + 1)
                copy(y_sb[:, tile_cols(t)], y_sum(t)).then_inc(s_moved, 1)

            def one_hot_tail(h):
                act.wait_ge(s_hot_ids[h], 16)
                if h >= 1:
                    act.wait_ge(s_onehot_used, HC * h)
                x = onehot[:, TAIL, :]
                nc.scalar.activation(x, hot_ids[:, h, :], ACT.Abs, bias=minus_row[:, :]).then_inc(s_distance, 1)
                act.wait_ge(s_distance, h + 1)
                nc.scalar.activation(x, x.bitcast(F32), ACT.Relu, bias=one_col[:, :],
                                     scale=-1.0).then_inc(s_onehot_tail, 1)

            act.wait_ge(s_ident, 1)
            zero(features_T[:, :, NF:SLOTS])
            for step, *a in STEPS:
                if step == "rows":
                    split_table(0)
                    bias_rows()
                    act.wait_ge(s_row_number, 3)
                    one_hot_tail(0)
                    act.wait_ge(s_moved, 1)
                    split_table(1)
                elif step == "dense":
                    dense_features()
                elif step == "hot":
                    if a[0] + 1 < NHOT:
                        one_hot_tail(a[0] + 1)
                    if a[0] + 2 < NHOT:
                        split_table(a[0] + 2)
                    move_hot(a[0])
                    if a[0] in range(2, 2 + NG - EARLY_GROUPS):
                        zero(group_view(LAST, EARLY_GROUPS + a[0] - 2))
                elif step == "group":
                    move_group(*a)
                elif step == "spread":
                    spread(act, 0, copy, *a)
                elif step == "layer1" and a[1] == chunks_of[a[0]][-1]:
                    for c in range(0, C1, 2):
                        relu_h1(a[0], c)
                elif step == "layer2":
                    relu_h2(*a)
                elif step == "layer3":
                    move_y(*a)

        @block.vector
        def _(dve):
            copy = nc.vector.tensor_copy

            def one_hot(h):
                dve.wait_ge(s_hot_ids[h], 16)
                for c in range(TAIL):
                    if h:
                        dve.wait_ge(s_onehot_used, HC * (h - 1) + c + 1)
                    nc.vector.tensor_scalar(onehot[:, c, :], hot_ids[:, h, :], row_number[:, c:c + 1], None,
                                            ALU.is_equal).then_inc(s_onehot, 1)

            def low_part(h):
                dve.wait_ge(s_hi, h + 1)
                nc.vector.tensor_tensor(table_lo[:, h % 2, :, :], table_sb[:, h % 2, :, :],
                                        table_hi[:, h % 2, :, :].bitcast(F32), ALU.subtract).then_inc(s_lo, 1)

            def relu(dst, src, bias):
                return nc.vector.tensor_scalar(dst, src, bias, 0.0, ALU.add, ALU.max)

            def relu_h1(t, c):
                dve.wait_ge(s_h1, C1 * t + c + 1)
                relu(h1_T[:, c, tile_cols(t)], h1_sum(c), b1_col[:, c:c + 1]).then_inc(s_h1_relu[1], 1)

            def relu_h2(t):
                dve.wait_ge(s_h2, C2 * t + 2)
                relu(h2_T[:, 1, tile_cols(t)], h2_sum(1), b2_col[:, 1:2]).then_inc(s_h2_relu[1], 1)

            dve.wait_ge(s_row_number_int, 1)
            copy(row_number[:, :], row_number_int[:, :]).then_inc(s_row_number, 1)
            nc.vector.tensor_scalar(minus_row[:, :], row_number_int[:, TAIL:HC], -1.0, None,
                                    ALU.mult).then_inc(s_row_number, 1)
            nc.vector.memset(one_col[:, :], 1.0).then_inc(s_row_number, 1)
            nc.vector.memset(w1_pairs[:, :, :], 0.0).then_inc(s_w1_zeroed, 1)
            nc.vector.memset(w1_packed[:, :], 0.0).then_inc(s_w1_zeroed, 1)
            nc.vector.memset(pairs_T[SLOTS * (COLS % QUADS):P, CHUNKS - 1, :], 0.0).then_inc(s_end_zeroed, 1)
            dve.wait_ge(s_row_number, 1)
            one_hot(0)
            low_part(0)
            for step, *a in STEPS:
                if step == "hot":
                    if a[0] + 1 < NHOT:
                        low_part(a[0] + 1)
                        one_hot(a[0] + 1)
                    if a[0] == NHOT - 1:
                        dve.wait_ge(s_w1_ends, 32)
                        nc.vector.tensor_tensor(w1_dense[:, :], w1_dense[:, :], w1_back[:, :],
                                                ALU.add).then_inc(s_w1_summed, 1)
                elif step == "spread":
                    spread(dve, 1, copy, *a)
                elif step == "layer1" and a[1] == chunks_of[a[0]][-1]:
                    for c in range(1, C1, 2):
                        relu_h1(a[0], c)
                elif step == "layer2":
                    relu_h2(*a)

        @block.tensor
        def _(pe):
            def bias_rows():
                pe.wait_ge(s_ident, 1)
                pe.wait_ge(s_rows, 48)
                nc.tensor.transpose(turn_ps[:, 0, 0, 0:ROWS], rows_sb[:, :], ident[0:ROWS, 0:ROWS]).then_inc(s_turned, 1)

            def dense_features():
                pe.wait_ge(s_dense, 16)
                for t in range(TILES):
                    last = nc.tensor.transpose(turn_ps[:, turn("dense") % 2, t, :], dense_sb[:, t, :], ident[:, :])
                last.then_inc(s_turned, 1)

            def look_up(h):
                pe.wait_ge(s_hi, h + 1)
                if h >= 2:
                    pe.wait_ge(s_hot_moved, h - 1)
                hi, lo = (table_hi, True, False), (table_lo, False, True)
                for parts in [[hi], [lo]] if h == 0 else [[hi, lo]]:
                    for c in range(HC):
                        for part, first, final in parts:
                            if first and c < TAIL:
                                pe.wait_ge(s_onehot, TAIL * h + c + 1)
                            elif first:
                                pe.wait_ge(s_onehot_tail, h + 1)
                            elif c == 0:
                                pe.wait_ge(s_lo, h + 1)
                            last = nc.tensor.matmul(mlp_ps[:, h % 2, :], part[:, h % 2, c, :], onehot[:, c, :],
                                                    start=(c == 0 and first), stop=(c == TAIL and final))
                        if final:
                            last.then_inc(s_onehot_used, 1)

            def turn_group(t, g):
                k = turn("group", t, g)
                pe.wait_ge(s_gathered[t][g], 16 * len(group_slots[g]))
                pe.wait_ge(s_moved, k - 1)
                for i, s in enumerate(group_slots[g]):
                    last = nc.tensor.transpose(turn_ps[:, k % 2, i, :], gathered[:, t, place[s], :], ident[:, :])
                last.then_inc(s_turned, 1)

            def multiply_pairs(p, part):
                if p == 0 and part == 0:
                    pe.wait_ge(s_pads, N_PADS)
                    pe.wait_ge(s_hot_moved, NHOT)
                if part == 0:
                    t, g = {EARLY: (LAST, EARLY_GROUPS - 1), LATE: (LAST, NG - 1)}.get(p, (p, NG - 1))
                    pe.wait_ge(s_moved, turn("group", t, g) + 1)
                half = part // 2
                if p >= 2 and part % 2 == 0:
                    wait_spread(pe, moved_halves(p - 1, half))
                n = PER_QUAD // PARTS
                for i in range(n):
                    for j in range(QUADS):
                        x = features_T[:, min(p, LAST) * P + j * PER_QUAD + n * part + i, :]
                        place = n * (part % 2) + i
                        last = nc.tensor.matmul(dots_view(p, half)[SLOTS * j:SLOTS * (j + 1), place, 0:COLS],
                                                x, x[:, 0:COLS], start=True, stop=True)
                if part % 2:
                    last.then_inc(s_dots, 1)

            def wait_h1_relu(t, c):
                pe.wait_ge(s_h1_relu[c % 2], h1_relu_count(t, c))

            def wait_h1_bank(t, c):
                if c < C2:
                    if t:
                        pe.wait_ge(s_h2_relu[c], t)
                elif t == 0:
                    wait_spread(pe, moved_halves(0, c - C2))
                else:
                    wait_h1_relu(t - 1, c)

            def layer1(t, q):
                first, final = q == chunks_of[t][0], q == chunks_of[t][-1]
                if t == 0 and q == "dense":
                    pe.wait_ge(s_w1_summed, 1)
                if t == 0 and q == 0:
                    pe.wait_ge(s_w1_pairs, 16 * COLS)
                if q == 0:
                    wait_spread(pe, moved_halves(LATE if t == LAST else t))
                if q == "packed":
                    pe.wait_ge(s_packed[t], 16 * (CHUNKS - WIDE))
                for c in [*range(C2, C1), *range(C2)] if first and t else range(C1):
                    if first:
                        wait_h1_bank(t, c)
                    if q == "dense":
                        w, x = w1_dense, dense_T
                    elif q == "packed":
                        w, x = w1_packed, packed_T
                    else:
                        w, x = w1_pairs[:, q, :], pairs_T[:, q, :]
                    last = nc.tensor.matmul(h1_sum(c), w[:, c * P:(c + 1) * P], x[:, tile_cols(t)],
                                            start=first, stop=final)
                    if final:
                        last.then_inc(s_h1, 1)

            def layer2(t):
                if t == 0:
                    pe.wait_ge(s_w2, 16)
                for m in range(C2):
                    for c in range(C1):
                        if m == 0:
                            wait_h1_relu(t, c)
                        last = nc.tensor.matmul(h2_sum(m), w2_sb[:, c, m * P:(m + 1) * P], h1_T[:, c, tile_cols(t)],
                                                start=(c == 0), stop=(c == C1 - 1))
                    last.then_inc(s_h2, 1)

            def layer3(t):
                pe.wait_ge(s_moved, turn("layer3", t) - 1)
                for m in range(C2):
                    pe.wait_ge(s_h2_relu[m], t + 1)
                    last = nc.tensor.matmul(y_sum(t), w3_col[:, m:m + 1], h2_T[:, m, tile_cols(t)],
                                            start=(m == 0), stop=(m == C2 - 1))
                last.then_inc(s_turned, 1)

            for step, *a in STEPS:
                if step == "rows":
                    bias_rows()
                elif step == "dense":
                    dense_features()
                elif step == "hot":
                    look_up(*a)
                elif step == "group":
                    turn_group(*a)
                elif step == "pairs":
                    multiply_pairs(*a)
                elif step == "layer1":
                    layer1(*a)
                elif step == "layer2":
                    layer2(*a)
                elif step == "layer3":
                    layer3(*a)


_TABLES = [f"tbl_{i}" for i in range(26)]
_WEIGHTS = ["W_top1", "b_top1", "W_top2", "b_top2", "W_top3"]


def kernel(**inputs):
    import numpy as _np
    import concourse.bacc as _bacc
    from concourse import mybir as _mybir
    from concourse.bass_utils import run_bass_kernel_spmd as _run

    nc = _bacc.Bacc("TRN2", target_bir_lowering=False, num_devices=1)
    arrays, aps = {}, {}
    for name in ["r_dense_features", "ids"] + _TABLES + _WEIGHTS:
        a = _np.ascontiguousarray(inputs[name])
        arrays[f"in_{name}_dram"] = a
        aps[name] = nc.dram_tensor(f"in_{name}_dram", a.shape, _mybir.dt.from_np(a.dtype), kind="ExternalInput").ap()
    ids_T = _np.ascontiguousarray(inputs["ids"].T)
    arrays["in_ids_T_dram"] = ids_T
    aps["ids_T"] = nc.dram_tensor("in_ids_T_dram", ids_T.shape, _mybir.dt.from_np(ids_T.dtype), kind="ExternalInput").ap()
    out = nc.dram_tensor("out_0_dram", (512, 1), _mybir.dt.float32, kind="ExternalOutput").ap()
    dlrm_tower(nc, aps["r_dense_features"], aps["ids"], aps["ids_T"], [aps[n] for n in _TABLES], *[aps[n] for n in _WEIGHTS], out)
    r = _run(nc, [arrays], core_ids=[0])
    return r.results[0]["out_0_dram"]
```
